# Optimizing a Trainium2 kernel written in Bass

```python
import numpy as np
import jax
import jax.numpy as jnp

def _softmax(x, axis=-1):
    return jax.nn.softmax(x, axis=axis)

def _gelu(x):
    return jax.nn.gelu(x, approximate=True)

def _silu(x):
    return jax.nn.silu(x)

def _sigmoid(x):
    return jax.nn.sigmoid(x)

def _layernorm(x, axis=-1, eps=1e-05):
    m = jnp.mean(x, axis=axis, keepdims=True)
    v = jnp.var(x, axis=axis, keepdims=True)
    return (x - m) / jnp.sqrt(v + eps)

def _scatter_add(tgt, idx, src, axis=0):
    return tgt.at[idx].add(src)

def _segment_sum(src, seg, n):
    return jax.ops.segment_sum(src, seg, n)
kernel_name = 'mk_gnn_preln_d2_gnn_r8_4353bd'

def setup_inputs(seed: int=0):
    np.random.seed(seed)
    _w = jnp.asarray

    def _rec_inputs():
        import jax
        import jax.numpy as jnp
        _gk = jax.random.key(seed)
        x = -0.0003019 + 1 * jax.random.normal(jax.random.fold_in(_gk, 1), (2500, 1024), jnp.float32)
        src = jax.random.randint(jax.random.fold_in(_gk, 2), (80000,), 0, 2500, jnp.int32)
        dst = jax.random.randint(jax.random.fold_in(_gk, 3), (80000,), 0, 2500, jnp.int32)
        _o = jnp.argsort(dst, stable=True)
        src = src[_o]
        dst = dst[_o]
        edge_weight = -0.000130211 + 0.031236 * jax.random.normal(jax.random.fold_in(_gk, 13), (80000,), jnp.float32)
        return (x, src, dst, edge_weight)
    x, src, dst, edge_weight = _rec_inputs()

    def _L0_gnn_setup():
        import jax, jax.numpy as jnp
        import numpy as np
        N, IN_FEAT, OUT_FEAT, HEADS, E = (2500, 1024, 256, 4, 40000)
        NEG_SLOPE = 0.2
        key = jax.random.key(seed)
        k1, k2, k3, k4, k5, k6 = jax.random.split(key, 6)
        h = jax.random.normal(k1, (N, IN_FEAT), dtype=jnp.float32)
        src = jax.random.randint(k2, (E,), 0, N, dtype=jnp.int32)
        dst = jax.random.randint(k3, (E,), 0, N, dtype=jnp.int32)
        W = jax.random.normal(k4, (HEADS, IN_FEAT, OUT_FEAT), dtype=jnp.float32) * (1.0 / np.sqrt(IN_FEAT))
        a_l = jax.random.normal(k5, (HEADS, OUT_FEAT), dtype=jnp.float32) * (1.0 / np.sqrt(OUT_FEAT))
        a_r = jax.random.normal(k6, (HEADS, OUT_FEAT), dtype=jnp.float32) * (1.0 / np.sqrt(OUT_FEAT))
        return {'h': h, 'W': W, 'a_l': a_l, 'a_r': a_r, 'src': src, 'dst': dst}
    _L0_gnn_all = _L0_gnn_setup()
    _L0_gnn_in = {k: v for k, v in _L0_gnn_all.items() if k in ('W', 'a_l', 'a_r')}
    del _L0_gnn_all

    def _L1_gnn_setup():
        import jax, jax.numpy as jnp
        import numpy as np
        INDIM = 1024
        OUTDIM = 1024
        NNZ = 8192
        N = 6250
        key = jax.random.key(seed)
        k1, k2, k3, k4, k5 = jax.random.split(key, 5)
        x = jax.random.normal(k1, (N, INDIM), dtype=jnp.float32)
        stdv = np.sqrt(6.0 / (INDIM + OUTDIM))
        nnz_weight = jax.random.uniform(k2, (NNZ,), dtype=jnp.float32, minval=-stdv, maxval=stdv)
        bias = jax.random.normal(k3, (OUTDIM,), dtype=jnp.float32) * 0.02
        row = jax.random.randint(k4, (NNZ,), 0, OUTDIM, dtype=jnp.int64)
        col = jax.random.randint(k5, (NNZ,), 0, INDIM, dtype=jnp.int64)
        edge_index = jnp.stack([row, col])
        return {'x': x, 'nnz_weight': nnz_weight, 'bias': bias, 'edge_index': edge_index}
    _L1_gnn_all = _L1_gnn_setup()
    _L1_gnn_in = {k: v for k, v in _L1_gnn_all.items() if k in ('bias',)}
    del _L1_gnn_all
    return {'x': x, 'src': src, 'dst': dst, 'edge_weight': edge_weight, 'L0_gnn_W': _L0_gnn_in['W'], 'L0_gnn_a_l': _L0_gnn_in['a_l'], 'L0_gnn_a_r': _L0_gnn_in['a_r'], 'L1_gnn_bias': _L1_gnn_in['bias']}

def reference(x, src, dst, edge_weight, L0_gnn_W, L0_gnn_a_l, L0_gnn_a_r, L1_gnn_bias):
    import jax
    import jax.numpy as jnp

    def _L0_gnn_ref(h, W, a_l, a_r, src, dst):
        import jax, jax.numpy as jnp
        import numpy as np
        N, IN_FEAT, OUT_FEAT, HEADS, E = (2500, 1024, 256, 4, 40000)
        NEG_SLOPE = 0.2
        z = jnp.einsum('ni,hif->nhf', h, W)
        el = jnp.einsum('nhf,hf->nh', z, a_l)
        er = jnp.einsum('nhf,hf->nh', z, a_r)
        e = jax.nn.leaky_relu(el[src] + er[dst], NEG_SLOPE)
        m = jax.ops.segment_max(e, dst, num_segments=N)
        ex = jnp.exp(e - m[dst])
        s = jax.ops.segment_sum(ex, dst, num_segments=N)
        alpha = ex / s[dst]
        out = jax.ops.segment_sum(alpha[:, :, None] * z[src], dst, num_segments=N)
        return out.reshape(N, HEADS * OUT_FEAT)

    def _L1_gnn_ref(x, nnz_weight, bias, edge_index):
        import jax, jax.numpy as jnp
        import numpy as np
        INDIM = 1024
        OUTDIM = 1024
        NNZ = 8192
        N = 6250
        row, col = (edge_index[0], edge_index[1])
        W = jnp.zeros((OUTDIM, INDIM), dtype=nnz_weight.dtype).at[row, col].add(nnz_weight)
        return x @ W.T + bias
    edge_index = jnp.stack([src, dst])
    h = jnp.maximum(_layernorm(x, axis=-1), 0.0)
    x = x + _L0_gnn_ref(h, L0_gnn_W, L0_gnn_a_l, L0_gnn_a_r, src, dst)
    h = jnp.maximum(_layernorm(x, axis=-1), 0.0)
    x = x + _L1_gnn_ref(h, edge_weight, L1_gnn_bias, edge_index)
    return x

_drawn_inputs = setup_inputs


def setup_inputs(seed=0):
    import zlib

    import numpy as np

    out = dict(_drawn_inputs(seed))
    spreads = {}
    factors = {'L0_gnn_a_r': 3.599, 'L1_gnn_bias': 3.009}
    for name, (base, spread) in spreads.items():
        noise = np.random.default_rng([zlib.crc32(name.encode()), seed]).standard_normal(out[name].shape)
        drawn = base * np.exp(spread * noise) if base else spread * noise
        out[name] = jnp.asarray(drawn.astype(out[name].dtype))
    for name, factor in factors.items():
        out[name] = (out[name] * factor).astype(out[name].dtype)
    return out
```

```python
import concourse.bass as bass
from concourse import mybir
from contextlib import ExitStack

FP32, BF16, FP16 = mybir.dt.float32, mybir.dt.bfloat16, mybir.dt.float16
I32, U32 = mybir.dt.int32, mybir.dt.uint32
ALU, ACT, AX = mybir.AluOpType, mybir.ActivationFunctionType, mybir.AxisListType

P = 128
N, D, E = 2500, 1024, 80000
HEADS, F = 4, 256
KD = D // P
TILES = -(-N // P)
LAST = N - (TILES - 1) * P
SUB = 32
SPB = P // SUB
NSUB = TILES * SPB
C = 9
WIN = C * P
GROUPS = 3
GCH = C // GROUPS
COLS = E // P
GC = 5
GSTEPS = COLS // GC
WBLOCKS = D // P
NWSUB = WBLOCKS * SPB
ROW = D + HEADS
SUBPAD = NSUB + 4
FARSRC = 1 << 20
MASKED = -1.0e30
FLOOR = -1.0e29
TINY = 1.0e-30
EPS = 1.0e-5
SLOPE = 0.2
RSQRT_MAGIC = 1597463007.0

NEWTON = 3
NORM_LINKS = 6 + 2 * NEWTON
PAIR_LINKS = 2 * (NORM_LINKS + 8)
SCORE_LINKS = 6 + 1
BLOCK_LINKS = SPB * SCORE_LINKS + NORM_LINKS + 6
G_WEIGHT_LINKS = 2
G_MAX_LINKS = 10
G_PROB_LINKS = 8
G_BLOCK_LINKS = SPB * (1 + GSTEPS * (G_MAX_LINKS + G_PROB_LINKS) + 1) + NORM_LINKS + 6


class Chain:

    def __init__(self, eng, sem, base=0):
        self.eng, self.sem, self.base, self.n = eng, sem, base, 0

    def link(self, ins):
        self.n += 1
        ins.then_inc(self.sem, 1)
        self.eng.wait_ge(self.sem, self.base + self.n)


def gnn_kernel(nc, x, src, dst, edge_weight, W, a_l, a_r, bias, out):
    with ExitStack() as ctx:
        def sb(name, shape, dt=FP32):
            return ctx.enter_context(nc.sbuf_tensor(name, shape, dt))

        def sem(name):
            return ctx.enter_context(nc.semaphore(name))

        zrows = nc.dram_tensor("zrows", [N, ROW], FP32).ap()
        er_d = nc.dram_tensor("er_d", [SUBPAD * SUB, HEADS], FP32).ap()

        rows = sb("rows", [P, 2, C, ROW])
        stage_w = rows[:, :, :, :].rearrange("p a c r -> p (a c r)")
        w_in = stage_w[:, 0:8192].rearrange("p (k n) -> p k n", k=KD)
        w_hi = stage_w[:, 8192:12288].bitcast(BF16).rearrange("p (k n) -> p k n", k=KD)
        w_lo = stage_w[:, 12288:16384].bitcast(BF16).rearrange("p (k n) -> p k n", k=KD)

        work = sb("work", [P, 7744])
        SC = C * HEADS * SUB

        def view4(t):
            return t.rearrange("p (c h d) -> p c h d", c=C, h=HEADS)
        score = view4(work[:, 0:SC])
        query = view4(work[:, SC:2 * SC])
        pairs = [work[:, (2 + 2 * i) * SC:(4 + 2 * i) * SC] for i in range(2)]
        prob = [t.rearrange("p (c h t d) -> p c h t d", c=C, h=HEADS, t=2)[:, :, :, 0, :] for t in pairs]
        upper = [t.bitcast(BF16).rearrange("p (c h x u) -> p c h x u", c=C, h=HEADS, u=2)[:, :, :, :, 1]
                 for t in pairs]
        outside = work[:, 6 * SC:6 * SC + C * SUB].rearrange("p (c d) -> p c d", c=C)
        rowmax = work[:, 7200:7328]
        diag = work[:, 7328:7456]
        group_max = work[:, 7456:7584]
        al_b, ar_b, junk = work[:, 3600:3600 + D], work[:, 6688:6688 + D], work[:, 4624:4624 + F]
        pick_src = [work[:, i * 512:(i + 1) * 512].bitcast(BF16) for i in range(4)]
        pick_dst = [work[:, 2048 + i * 432:2048 + (i + 1) * 432].bitcast(BF16).rearrange(
            "p (c j d) -> p c j d", c=C, j=3) for i in range(2)]
        iota_src = work[:, 5120:5632].bitcast(FP16)
        own = work[:, 5632:5632 + C * SUB].rearrange("p (c d) -> p c d", c=C)
        wres = work[:, 5952:5952 + NWSUB * C]
        wparts = work[:, 6240:6672].bitcast(BF16).rearrange("p (n j) -> p n j", j=3)
        wpart = [wparts[:, :, j] for j in range(3)]
        win_i = work[:, 0:NSUB * C].bitcast(I32)
        win_s = work[:, 720:1440].bitcast(I32)
        edges_i = work[:, 1440:1440 + COLS + 1].bitcast(I32)
        edges_f = work[:, 2080:2080 + COLS + 1]
        cmp = work[:, 2720:2720 + COLS + 1]
        w1_hi = sb("w1_hi", [P, KD, D], BF16)
        w1_lo = sb("w1_lo", [P, KD, D], BF16)

        xt = sb("xt", [P, D])
        yo = sb("yo", [P, D])
        xz = [xt, yo]
        osum = [sb(f"osum{i}", [P, ROW]) for i in range(2)]
        zt = osum
        hb = sb("hb", [P, D])
        part_sum = [osum[0][:, 0:D], osum[1][:, 0:D], hb[:, :]]
        wblock = yo[:, :]
        hT_hi = sb("hT_hi", [P, 2, D], BF16)
        hT_lo = sb("hT_lo", [P, 2, D], BF16)
        bias_b = sb("bias_b", [P, D])
        er_b = sb("er_b", [P, SPB, SUB * HEADS])
        dloc = sb("dloc", [P, SUBPAD * C])
        idx = sb("idx", [P, SUBPAD * C], U32)
        idxr = sb("idxr", [P, 2, C], U32)
        srcf = sb("srcf", [P, NWSUB * C])
        wwin = sb("wwin", [P, NWSUB * C])
        thr = sb("thr", [P, NSUB])
        first_q = sb("first_q", [P, NSUB, C])
        iota_d = sb("iota_d", [P, SUB])
        ident = sb("ident", [P, P])
        ones = sb("ones", [P, P])
        ones_b = sb("ones_b", [P, 2], BF16)
        stats = sb("stats", [P, 12])
        mv = sb("mv", [P, 2])
        rs = sb("rs", [P, 8])
        er_t = sb("er_t", [P, 8])
        den = sb("den", [P, 2 * HEADS])
        mx = sb("mx", [P, 4])
        cnt = sb("cnt", [P, 8])
        ge = sb("ge", [P, NSUB])
        notge = sb("notge", [P, NSUB])
        pick = sb("pick", [P, NSUB])
        starts_f = sb("starts_f", [1, NSUB + 1])
        diff = sb("diff", [1, NSUB + 8])
        starts = sb("starts", [1, NSUB], I32)
        flag = sb("flag", [1, 2], I32)

        spare = rows[:, 1, :, :].rearrange("p c r -> p (c r)")
        all_i = spare[:, 0:2 * COLS].bitcast(I32)
        all_dst, all_src, all_w, all_res = (spare[:, (2 + i) * COLS:(3 + i) * COLS] for i in range(4))
        all_part = [spare[:, 3760 + 320 * j:3760 + 320 * (j + 1)].bitcast(BF16)[:, 0:COLS] for j in range(3)]
        near = spare[:, 4800:4800 + 4 * GC]
        step_max = spare[:, 4840:4840 + P]
        zeros_b = hT_hi[:, 1, 0:512]

        acc = [ctx.enter_context(nc.psum_tensor(f"acc{i}", [P, 1024], FP32)) for i in range(2)]
        small = ctx.enter_context(nc.psum_tensor("small", [P, 512], FP32))
        turn = ctx.enter_context(nc.psum_tensor("turn", [P, 512], FP32))
        tb = [ctx.enter_context(nc.psum_tensor(f"tb{i}", [P, 512], FP32)) for i in range(2)]

        const_ready = sem("const_ready")
        dve_done = sem("dve_done")
        act_done = sem("act_done")
        pool_done = sem("pool_done")
        dve_turn = sem("dve_turn")
        edges_loaded = sem("edges_loaded")
        picks_ready = sem("picks_ready")
        rows_picked = sem("rows_picked")
        counts_ready = sem("counts_ready")
        counts_turned = sem("counts_turned")
        starts_ready = sem("starts_ready")
        windows_loaded = sem("windows_loaded")
        windows_ready = sem("windows_ready")
        vecs_loaded = sem("vecs_loaded")
        w_loaded = [sem(f"w_loaded{k}") for k in range(KD)]
        w_hi_ready = sem("w_hi_ready")
        w_lo_ready = sem("w_lo_ready")
        x_loaded = [sem(f"x_loaded{i}") for i in range(2)]
        z_ln_ready = sem("z_ln_ready")
        z_h_ready = sem("z_h_ready")
        z_hT_ready = sem("z_hT_ready")
        z_hi_ready = sem("z_hi_ready")
        z_lo_ready = sem("z_lo_ready")
        z_ready = sem("z_ready")
        z_top_ready = sem("z_top_ready")
        z_row_ready = sem("z_row_ready")
        z_stored = [sem(f"z_stored{i}") for i in range(2)]
        er_tail_stored = sem("er_tail_stored")
        pick_src_ready = sem("pick_src_ready")
        pick_dst_ready = sem("pick_dst_ready")
        picks_used = sem("picks_used")
        part_copied = sem("part_copied")
        parts_added = sem("parts_added")
        wblock_ready = sem("wblock_ready")
        w1_hi_ready = sem("w1_hi_ready")
        w1_lo_ready = sem("w1_lo_ready")
        ring_clear = sem("ring_clear")
        idx_ready = sem("idx_ready")
        gather_turn = sem("gather_turn")
        gathered = [[sem(f"gathered{i}_{g}") for g in range(GROUPS)] for i in range(2)]
        er_loaded = [sem(f"er_loaded{i}") for i in range(SPB)]
        outside_ready = sem("outside_ready")
        outside_scaled = sem("outside_scaled")
        query_ready = sem("query_ready")
        rowmax_ready = sem("rowmax_ready")
        rowmax_turned = sem("rowmax_turned")
        diag_ready = sem("diag_ready")
        max_spread = sem("max_spread")
        logits_ready = sem("logits_ready")
        exp_done = sem("exp_done")
        score_ready = sem("score_ready")
        prob_lo_ready = sem("prob_lo_ready")
        rows_used = sem("rows_used")
        acc_ready = sem("acc_ready")
        acc_taken = sem("acc_taken")
        xt_loaded = sem("xt_loaded")
        xt_free = sem("xt_free")
        osum_free = sem("osum_free")
        ln_ready = sem("ln_ready")
        h_ready = sem("h_ready")
        hT_ready = sem("hT_ready")
        hT_hi_ready = sem("hT_hi_ready")
        hT_lo_ready = sem("hT_lo_ready")
        y_ready = sem("y_ready")
        y_taken = sem("y_taken")
        out_stored = sem("out_stored")
        all_loaded = sem("all_loaded")
        all_ready = sem("all_ready")
        g_src_ready = sem("g_src_ready")
        g_dst_ready = sem("g_dst_ready")
        g_used = sem("g_used")
        g_part_ready = sem("g_part_ready")
        g_idx_ready = sem("g_idx_ready")
        g_gathered = sem("g_gathered")
        g_seen = sem("g_seen")
        g_cleared = sem("g_cleared")
        g_logits = sem("g_logits")
        g_exp = sem("g_exp")
        g_score = sem("g_score")
        g_prob_lo = sem("g_prob_lo")
        g_added = sem("g_added")
        g_block_free = sem("g_block_free")

        def fits(eng):
            eng.wait_ge(starts_ready, 1)
            return eng.value_load(flag[0:1, 0:1], min_val=0, max_val=1)

        block = ctx.enter_context(nc.Block())

        @block.sync
        def _(sp):
            sp.dma_start(edges_i[:, 1:COLS + 1], dst.rearrange("(p j) -> p j", p=P)).then_inc(edges_loaded, 16)
            sp.dma_start(edges_i[1:P, 0:1], dst.rearrange("(p j) -> p j", p=P)[0:P - 1, COLS - 1:COLS],
                         allow_slow_non_contiguous=True).then_inc(edges_loaded, 16)

            def load_x(t, slot, n=P):
                sp.dma_start(xz[slot][0:n, :], x[bass.ds(t * P, n), :]).then_inc(x_loaded[slot], 16)

            for t in range(2):
                load_x(t, t)
            for k in range(KD):
                sp.dma_start(w_in[:, k, :].rearrange("p (h f) -> p h f", h=HEADS),
                             W[:, k * P:(k + 1) * P, :].rearrange("h p f -> p h f")).then_inc(w_loaded[k], 16)
            sp.dma_start(al_b, a_l.rearrange("h f -> (h f)").partition_broadcast(P)).then_inc(vecs_loaded, 16)
            sp.dma_start(ar_b, a_r.rearrange("h f -> (h f)").partition_broadcast(P)).then_inc(vecs_loaded, 16)
            sp.dma_start(bias_b[:, :], bias.partition_broadcast(P)).then_inc(vecs_loaded, 16)

            def store_z(t, slot, n=P):
                sp.wait_ge(z_row_ready, t + 1)
                sp.dma_start(zrows[bass.ds(t * P, n), :], zt[slot][0:n, :]).then_inc(z_stored[slot], 16)
                sp.dma_start(er_d[bass.ds(t * P, P), :], er_t[:, slot * HEADS:(slot + 1) * HEADS]
                             ).then_inc(z_stored[slot], 16)

            def next_x(t, slot, ahead=P):
                sp.wait_ge(z_h_ready, t + 1)
                load_x(t + 2, slot, ahead)

            def project_dma(t, slot, ahead=P):
                next_x(t, slot, ahead)
                store_z(t - 2, slot)

            next_x(0, 0)
            next_x(1, 1)
            with sp.Fori(1, TILES // 2 - 2) as g:
                for s in range(2):
                    project_dma(2 * g + s, s)
            project_dma(TILES - 4, 0)
            project_dma(TILES - 3, 1, LAST)
            for t in range(TILES - 4, TILES - 1):
                store_z(t, t % 2)
            store_z(TILES - 1, 1, LAST)
            sp.dma_start(er_d[TILES * P:SUBPAD * SUB, :], ones[:, 0:HEADS]).then_inc(er_tail_stored, 16)
            sp.wait_ge(er_tail_stored, 16)

            sp.wait_ge(z_stored[0], 32 * (TILES // 2))
            sp.wait_ge(z_stored[1], 32 * (TILES // 2))

            def load_er(q, s):
                sp.dma_start(er_b[:, s, :], er_d[bass.ds(q * SUB, SUB), :].rearrange("d h -> (d h)")
                             .partition_broadcast(P)).then_inc(er_loaded[s], 16)

            def load_rows(b, n=P):
                sp.dma_start(xt[0:n, :], x[bass.ds(b * P, n), :]).then_inc(xt_loaded, 16)

            def store_rows(b, n=P):
                sp.wait_ge(y_taken, 2 * (b + 1))
                sp.dma_start(out[bass.ds(b * P, n), :], yo[0:n, :]).then_inc(out_stored, 16)

            def general_dma(b, n=P):
                sp.wait_ge(g_block_free, b + 1)
                for s in range(SPB):
                    load_er(SPB * b + s, s)
                load_rows(b, n)
                store_rows(b, n)

            fit = fits(sp)
            with sp.If(fit):
                for s in range(SPB):
                    load_er(s, s)
                load_rows(0)

                def attend_dma(b, first=False, second=False, last=False):
                    for s in range(SPB):
                        sp.wait_ge(query_ready, 4 * b + s + 1)
                        load_er(4 * b + s + SPB, s)
                        if s == 3 and not first and not second:
                            store_rows(b - 2)
                    if not first:
                        sp.wait_ge(xt_free, b)
                        load_rows(b, LAST if last else P)

                attend_dma(0, first=True)
                attend_dma(1, second=True)
                with sp.Fori(2, TILES - 1) as b:
                    attend_dma(b)
                attend_dma(TILES - 1, last=True)
                store_rows(TILES - 2)
                store_rows(TILES - 1, LAST)
            with sp.Else():
                for part, what in ((all_i[:, 0:COLS], dst), (all_i[:, COLS:], src), (all_w, edge_weight)):
                    sp.dma_start(part, what.rearrange("(p j) -> p j", p=P)).then_inc(all_loaded, 16)
                with sp.Fori(0, TILES - 1) as b:
                    general_dma(b)
                general_dma(TILES - 1, LAST)
            sp.wait_ge(out_stored, 16 * TILES)
            sp.wait_ge(er_tail_stored, 16)

        @block.gpsimd
        def _(pool):
            step = Chain(pool, pool_done)
            step.link(nc.gpsimd.memset(ones[:, :], 1.0))
            step.link(nc.gpsimd.memset(ident[:, :], 0.0))
            step.link(nc.gpsimd.affine_select(out=ident[:, :], in_=ident[:, :], compare_op=ALU.not_equal, fill=1.0,
                                              base=0, pattern=[[-1, P]], channel_multiplier=1))
            step.link(nc.gpsimd.memset(edges_i[0:1, 0:1], -1))
            step.link(nc.gpsimd.iota(thr[:, :], pattern=[[SUB, NSUB]], base=0, channel_multiplier=0,
                                     allow_small_or_imprecise_dtypes=True))
            step.link(nc.gpsimd.iota(first_q[:, :, :], pattern=[[SUB, NSUB], [0, C]], base=0, channel_multiplier=0,
                                     allow_small_or_imprecise_dtypes=True))
            step.link(nc.gpsimd.iota(iota_d[:, :], pattern=[[1, SUB]], base=0, channel_multiplier=0,
                                     allow_small_or_imprecise_dtypes=True))
            step.link(nc.gpsimd.iota(iota_src, pattern=[[1, D]], base=0, channel_multiplier=0,
                                     allow_small_or_imprecise_dtypes=True))
            step.link(nc.gpsimd.memset(ones_b[:, :], 1.0))
            step.link(nc.gpsimd.memset(dloc[:, NSUB * C:], -1.0))
            nc.gpsimd.memset(idx[:, NSUB * C:].bitcast(I32), FARSRC).then_inc(const_ready, 1)
            pool.wait_ge(starts_ready, 1)
            with pool.Fori(0, NSUB) as q:
                at = pool.value_load(starts[0:1, bass.ds(q, 1)], min_val=0, max_val=E - WIN)
                for part, what in ((win_i, dst), (win_s, src)):
                    pool.dma_start(part[:, bass.ds(q * C, C)],
                                   what[bass.ds(at, WIN)].rearrange("(p j) -> p j", j=C)
                                   ).then_inc(windows_loaded, 16)
            with pool.Fori(0, NWSUB) as q:
                at = pool.value_load(starts[0:1, bass.ds(q, 1)], min_val=0, max_val=E - WIN)
                pool.dma_start(wwin[:, bass.ds(q * C, C)],
                               edge_weight[bass.ds(at, WIN)].rearrange("(p j) -> p j", j=C)
                               ).then_inc(windows_loaded, 16)

            def add_parts(kb, first=False):
                pool.wait_ge(part_copied, SPB * (kb + 1))
                if not first:
                    pool.wait_ge(w1_lo_ready, 2 * kb)
                nc.gpsimd.tensor_tensor(wblock, part_sum[0], part_sum[1], ALU.add).then_inc(parts_added, 1)
                pool.wait_ge(parts_added, kb + 1)
                nc.gpsimd.tensor_tensor(wblock, wblock, part_sum[2], ALU.add).then_inc(wblock_ready, 1)

            def weights():
                add_parts(0, first=True)
                with pool.Fori(1, WBLOCKS) as kb:
                    add_parts(kb)

            limit = pool.to_reg(N - 1)
            pool.wait_ge(z_ready, TILES)
            pool.wait_ge(z_stored[0], 32 * (TILES // 2))
            pool.wait_ge(z_stored[1], 32 * (TILES // 2))

            def gather(q, s, reuse):
                sl = s % 2
                for c in range(C):
                    if c == 0:
                        pool.wait_ge(idx_ready, q + 1)
                        pool.sem_inc(gather_turn, 1)
                    if reuse:
                        pool.wait_ge(rows_used, C * (q - 2) + c + 1)
                        pool.sem_inc(gather_turn, 1)
                    pool.indirect_dma_start(rows[:, sl, c, :], None, zrows[:, :],
                                            bass.IndirectOffsetOnAxis(ap=idxr[:, sl, c:c + 1], axis=0),
                                            bounds_check=limit, oob_is_err=False
                                            ).then_inc(gathered[sl][c // GCH], 16)

            fit = fits(pool)
            with pool.If(fit):
                for s in range(2):
                    gather(s, s, False)
                weights()
                for s in range(2, SPB):
                    gather(s, s, True)
                with pool.Fori(1, TILES) as b:
                    for s in range(SPB):
                        gather(SPB * b + s, s, True)
            with pool.Else():
                weights()
                pool.sem_inc(g_cleared, 1)
                with pool.Fori(0, 2 * NSUB * GSTEPS) as n:
                    pool.wait_ge(g_idx_ready, n + 1)
                    pool.sem_inc(gather_turn, 1)
                    for c in range(GC):
                        pool.indirect_dma_start(rows[:, 0, c, :], None, zrows[:, :],
                                                bass.IndirectOffsetOnAxis(ap=idxr[:, 0, c:c + 1], axis=0),
                                                bounds_check=limit, oob_is_err=False).then_inc(g_gathered, 16)
                    pool.wait_ge(g_seen, n + 1)
                    pool.sem_inc(gather_turn, 1)
                    pool.inc_swdge_sem([g_gathered], [16 * GC], mode="sub").then_inc(g_cleared, 1)

        @block.vector
        def _(v):
            step = Chain(v, dve_done)

            def norm_stats(xs):
                for j in range(2):
                    step.link(nc.vector.bn_stats(stats[:, 6 * j:6 * j + 6], xs[:, 512 * j:512 * j + 512]))

            def norm(ready, count):
                v.sem_inc(dve_turn, 1)
                step.link(nc.vector.bn_aggr(mv[:, :], stats[:, :]))
                step.link(nc.vector.tensor_scalar(rs[:, 2:3], mv[:, 1:2], EPS, None, ALU.add))
                step.link(nc.vector.tensor_scalar(rs[:, 3:4].bitcast(I32), rs[:, 2:3].bitcast(I32), 1, None,
                                                  ALU.logical_shift_right))
                step.link(nc.vector.tensor_scalar(rs[:, 4:5].bitcast(I32), rs[:, 3:4].bitcast(I32), -1.0, RSQRT_MAGIC,
                                                  ALU.mult, ALU.add))
                factor = 1.0
                for i in range(NEWTON):
                    y, to = rs[:, 4 + i % 2:5 + i % 2], rs[:, 5 - i % 2:6 - i % 2]
                    step.link(nc.vector.scalar_tensor_tensor(rs[:, 6:7], y, rs[:, 2:3], y, ALU.mult, ALU.mult))
                    step.link(nc.vector.scalar_tensor_tensor(to, rs[:, 6:7], -3.0 * factor * factor, y,
                                                             ALU.add, ALU.mult))
                    factor = -2.0 * factor ** 3
                nc.vector.scalar_tensor_tensor(rs[:, 1:2], mv[:, 0:1], -1.0 / factor, to, ALU.mult, ALU.mult)
                nc.vector.tensor_scalar(rs[:, 0:1], to, 1.0 / factor, None, ALU.mult).then_inc(ready, 1)
                v.wait_ge(ready, count)

            def z_norm(t, slot, use):
                v.wait_ge(x_loaded[slot], 16 * use)
                if not isinstance(t, int) or t > 0:
                    v.wait_ge(z_h_ready, t)
                norm_stats(xz[slot][:, :])
                norm(z_ln_ready, t + 1)

            def z_lo(t, slot):
                v.wait_ge(z_hi_ready, 2 * (t + 1))
                if not isinstance(t, int) or t > 1:
                    v.wait_ge(z_ready, t - 1)
                for j in range(2):
                    ins = nc.vector.tensor_tensor(hT_lo[:, slot, 512 * j:512 * j + 512], tb[j][:, :],
                                                  hT_hi[:, slot, 512 * j:512 * j + 512], ALU.subtract)
                    ins.then_inc(z_lo_ready, 1)
                    v.wait_ge(z_lo_ready, 2 * t + j + 1)

            def z_post(t, slot, use):
                v.wait_ge(z_top_ready, t + 1)
                if not isinstance(use, int) or use > 1:
                    v.wait_ge(z_stored[slot], 32 * (use - 1))
                step.link(nc.vector.tensor_tensor(zt[slot][:, 512:1024].bitcast(BF16), acc[slot][:, :],
                                                  zt[slot][:, 0:512].bitcast(BF16), ALU.subtract))
                for vec, to in ((al_b, zt[slot][:, D:D + HEADS]), (ar_b, er_t[:, slot * HEADS:(slot + 1) * HEADS])):
                    for h in range(HEADS):
                        ins = nc.vector.tensor_tensor_reduce(
                            out=junk[:, 0:F], in0=acc[slot][:, h * F:(h + 1) * F], in1=vec[:, h * F:(h + 1) * F],
                            scale=1.0, scalar=0.0, op0=ALU.mult, op1=ALU.add, accum_out=to[:, h:h + 1])
                        if vec is ar_b and h == HEADS - 1:
                            ins.then_inc(z_row_ready, 1)
                            v.wait_ge(z_row_ready, t + 1)
                        else:
                            step.link(ins)

            def w_rest(k0, k1):
                for k in range(k0, k1):
                    v.wait_ge(w_hi_ready, k + 1)
                    nc.vector.tensor_tensor(w_lo[:, k, :], w_in[:, k, :], w_hi[:, k, :], ALU.subtract
                                            ).then_inc(w_lo_ready, 1)

            z_norm(0, 0, 1)
            z_norm(1, 1, 1)
            v.wait_ge(const_ready, 1)
            v.wait_ge(edges_loaded, 32)
            step.link(nc.vector.tensor_copy(edges_f, edges_i))
            step.link(nc.vector.tensor_scalar(ge[:, :], thr[:, :], edges_f[:, COLS:COLS + 1], None, ALU.is_le))
            step.link(nc.vector.tensor_scalar(notge[:, :], ge[:, :], -float(COLS), float(COLS), ALU.mult, ALU.add))
            step.link(nc.vector.scalar_tensor_tensor(pick[:, :], thr[:, :], edges_f[:, 0:1], ge[:, :],
                                                     ALU.is_gt, ALU.mult))
            step.link(nc.vector.tensor_tensor(cmp[:, 0:COLS], edges_f[:, 0:COLS], edges_f[:, 1:COLS + 1], ALU.is_gt))
            nc.vector.reduce_sum(cnt[:, 0:1], cmp[:, 0:COLS], AX.X).then_inc(picks_ready, 1)
            w_rest(0, 2)
            z_lo(0, 0)
            v.wait_ge(rows_picked, 1)
            step.link(nc.vector.tensor_scalar(cnt[0:NSUB, 2:3], small[0:NSUB, 0:1], 1.0, None, ALU.mult))
            step.link(nc.vector.tensor_scalar(cnt[0:NSUB, 3:4], small[0:NSUB, 8:9], 1.0, None, ALU.mult))
            step.link(nc.vector.tensor_scalar(cmp[0:NSUB, 0:COLS], acc[0][0:NSUB, 0:COLS], cnt[0:NSUB, 3:4], None,
                                              ALU.is_lt, ALU.add, accum_out=cnt[0:NSUB, 1:2]))
            step.link(nc.vector.tensor_tensor(cnt[0:NSUB, 2:3], cnt[0:NSUB, 2:3], cnt[0:NSUB, 1:2], ALU.add))
            nc.vector.tensor_scalar(cnt[0:NSUB, 2:3], cnt[0:NSUB, 2:3], float(E), None, ALU.min
                                    ).then_inc(counts_ready, 1)
            w_rest(2, 3)
            v.wait_ge(counts_turned, 1)
            step.link(nc.vector.tensor_copy(starts_f[0:1, 0:NSUB], turn[0:1, 0:NSUB]))
            step.link(nc.vector.memset(starts_f[0:1, NSUB:NSUB + 1], float(E)))
            step.link(nc.vector.tensor_tensor(diff[0:1, 0:NSUB], starts_f[0:1, 1:NSUB + 1], starts_f[0:1, 0:NSUB],
                                              ALU.subtract))
            step.link(nc.vector.reduce_max(diff[0:1, NSUB:NSUB + 1], diff[0:1, 0:NSUB], AX.X))
            step.link(nc.vector.tensor_scalar(diff[0:1, NSUB + 1:NSUB + 2], turn[0:1, 128:129], 0.0, None,
                                              ALU.is_equal))
            step.link(nc.vector.scalar_tensor_tensor(flag[0:1, 0:1], diff[0:1, NSUB:NSUB + 1], float(WIN),
                                                     diff[0:1, NSUB + 1:NSUB + 2], ALU.is_le, ALU.mult))
            nc.vector.tensor_scalar(starts[0:1, :], starts_f[0:1, 0:NSUB], float(E - WIN), None, ALU.min
                                    ).then_inc(starts_ready, 1)
            v.wait_ge(starts_ready, 1)

            w_rest(3, KD)
            v.wait_ge(vecs_loaded, 48)
            z_norm(2, 0, 2)
            z_lo(1, 1)

            def z_pair(g):
                for s in range(2):
                    t = 2 * g + s
                    z_norm(t + 1, 1 - s, g + 1 + s)
                    z_lo(t, s)
                    z_post(t - 2, s, g)

            z_pair(1)
            outer, n0 = step, step.n
            with v.Fori(2, TILES // 2 - 1) as g:
                step = Chain(v, dve_done, n0 + (g - 2) * PAIR_LINKS)
                z_pair(g)
                assert step.n == PAIR_LINKS, step.n
            step = outer
            step.n = n0 + PAIR_LINKS * (TILES // 2 - 3)
            z_norm(TILES - 1, 1, TILES // 2)
            z_lo(TILES - 2, 0)
            z_post(TILES - 4, 0, TILES // 2 - 1)
            z_lo(TILES - 1, 1)
            z_post(TILES - 3, 1, TILES // 2 - 1)

            v.wait_ge(windows_loaded, 16 * (2 * NSUB + NWSUB))
            step.link(nc.vector.tensor_copy(dloc[:, 0:NSUB * C], win_i))
            step.link(nc.vector.tensor_tensor(dloc[:, 0:NSUB * C], dloc[:, 0:NSUB * C],
                                              first_q[:, :, :].rearrange("p q c -> p (q c)"), ALU.subtract))
            step.link(nc.vector.tensor_copy(srcf[:, :], win_s[:, 0:NWSUB * C]))
            far = work[:, 1440:1440 + NSUB * C]
            far2 = work[:, 2880:2880 + NSUB * C]
            step.link(nc.vector.tensor_scalar(far, dloc[:, 0:NSUB * C], 0.0, float(FARSRC), ALU.is_lt, ALU.mult))
            step.link(nc.vector.tensor_scalar(far2, dloc[:, 0:NSUB * C], float(SUB - 1), float(FARSRC),
                                              ALU.is_gt, ALU.mult))
            step.link(nc.vector.tensor_tensor(far, far, far2, ALU.add))
            step.link(nc.vector.tensor_copy(idx[:, 0:2 * C], win_s[:, 0:2 * C]))
            nc.vector.tensor_tensor(idx[:, 2 * C:NSUB * C], win_s[:, 2 * C:], far[:, 2 * C:], ALU.add
                                    ).then_inc(windows_ready, 1)
            v.wait_ge(windows_ready, 1)
            for q in range(2):
                nc.vector.tensor_copy(idxr[:, q, :], idx[:, q * C:(q + 1) * C]).then_inc(idx_ready, 1)

            z_post(TILES - 2, 0, TILES // 2)

            def split_weights(whole, part, rest):
                step.link(nc.vector.tensor_copy(part[0], whole))
                step.link(nc.vector.tensor_tensor(rest, whole, part[0], ALU.subtract))
                step.link(nc.vector.tensor_copy(part[1], rest))
                step.link(nc.vector.tensor_tensor(rest, rest, part[1], ALU.subtract))
                step.link(nc.vector.tensor_copy(part[2], rest))

            split_weights(wwin[:, :], wpart, wres)
            z_post(TILES - 1, 1, TILES // 2)

            def weights_lo(kb):
                v.wait_ge(w1_hi_ready, 2 * (kb + 1))
                for j in range(2):
                    cols = slice(512 * j, 512 * j + 512)
                    nc.vector.tensor_tensor(w1_lo[:, bass.ds(kb, 1), cols], wblock[:, cols].unsqueeze(1),
                                            w1_hi[:, bass.ds(kb, 1), cols], ALU.subtract).then_inc(w1_lo_ready, 1)

            def weights_block(kb, first=False):
                for s in range(SPB):
                    q = SPB * kb + s
                    step.link(nc.vector.tensor_tensor(
                        own, iota_d[:, None, :].to_broadcast([P, C, SUB]),
                        dloc[:, bass.ds(q * C, C)].unsqueeze(2).to_broadcast([P, C, SUB]), ALU.is_equal))
                    if not first or s >= 2:
                        v.wait_ge(picks_used, C * (q - 1))
                    nc.vector.tensor_tensor(
                        pick_dst[s % 2], own.unsqueeze(2).to_broadcast([P, C, 3, SUB]),
                        wparts[:, bass.ds(q * C, C), :].unsqueeze(3).to_broadcast([P, C, 3, SUB]), ALU.mult
                    ).then_inc(pick_dst_ready, 1)
                    for c in range(C):
                        n = C * q + c
                        if not first or C * s + c >= 4:
                            v.wait_ge(picks_used, n - 3)
                        nc.vector.tensor_scalar(pick_src[(C * s + c) % 4], iota_src, srcf[:, bass.ds(n, 1)], None,
                                                ALU.is_equal).then_inc(pick_src_ready, 1)
                    if s == 2 and not first:
                        weights_lo(kb - 1)

            def take_idx(q, s):
                nc.vector.tensor_copy(idxr[:, s % 2, :], idx[:, bass.ds(q * C, C)]).then_inc(idx_ready, 1)

            def make_outside(q):
                nc.vector.tensor_tensor(
                    outside, iota_d[:, None, :].to_broadcast([P, C, SUB]),
                    dloc[:, bass.ds(q * C, C)].unsqueeze(2).to_broadcast([P, C, SUB]), ALU.not_equal
                ).then_inc(outside_ready, 1)

            def make_query(q, s, use):
                v.wait_ge(er_loaded[s], 16 * use)
                v.wait_ge(outside_scaled, q + 1)
                nc.vector.tensor_tensor(
                    query, outside.unsqueeze(2).to_broadcast([P, C, HEADS, SUB]),
                    er_b[:, s, :].rearrange("p (d h) -> p h d", h=HEADS).unsqueeze(1).to_broadcast(
                        [P, C, HEADS, SUB]), ALU.add).then_inc(query_ready, 1)
                v.wait_ge(query_ready, q + 1)

            def spread_diag(q):
                v.wait_ge(rowmax_turned, q + 1)
                step.link(nc.vector.reduce_max(mx[:, 0:1], turn[:, 0:P], AX.X))
                nc.vector.tensor_scalar(diag, ident[:, :], mx[:, 0:1], None, ALU.mult).then_inc(diag_ready, 1)
                v.wait_ge(diag_ready, q + 1)

            def scores(b, s):
                q, sl = SPB * b + s, s % 2
                for cs, to in ((slice(0, C - GCH), rowmax), (slice(C - GCH, C), group_max)):
                    for g in range(cs.start // GCH, cs.stop // GCH):
                        v.wait_ge(gathered[sl][g], 16 * GCH * (2 * b + s // 2 + 1))
                    if cs.stop == C:
                        take_idx(q + 2, s)
                    el = rows[:, sl, cs, D:ROW].unsqueeze(3).to_broadcast([P, cs.stop - cs.start, HEADS, SUB])
                    step.link(nc.vector.tensor_tensor(score[:, cs], query[:, cs], el, ALU.add))
                    step.link(nc.vector.scalar_tensor_tensor(score[:, cs], score[:, cs], SLOPE, score[:, cs],
                                                             ALU.mult, ALU.max))
                    step.link(nc.vector.tensor_reduce(to, score[:, cs].rearrange("p c h d -> p (h d) c"),
                                                      AX.X, ALU.max))
                nc.vector.scalar_tensor_tensor(rowmax, rowmax, FLOOR, group_max, ALU.max, ALU.max
                                               ).then_inc(rowmax_ready, 1)
                make_outside(q + 1)

            def weigh(b, s):
                q, sl = SPB * b + s, s % 2
                spread_diag(q)
                v.wait_ge(max_spread, q + 1)
                for g in range(GROUPS + 2):
                    cs, before = slice(g * GCH, (g + 1) * GCH), slice((g - 2) * GCH, (g - 1) * GCH)
                    if g < GROUPS:
                        nc.vector.tensor_tensor(
                            score[:, cs], score[:, cs],
                            turn[:, P:2 * P].rearrange("p (h d) -> p h d", h=HEADS).unsqueeze(1).to_broadcast(
                                [P, GCH, HEADS, SUB]), ALU.subtract).then_inc(logits_ready, 1)
                    if g >= 2:
                        v.wait_ge(exp_done, GROUPS * q + g - 1)
                        nc.vector.tensor_tensor(upper[sl][:, before, :, SUB:], prob[sl][:, before],
                                                upper[sl][:, before, :, 0:SUB], ALU.subtract
                                                ).then_inc(prob_lo_ready, 1)
                make_query(q + 1, (s + 1) % SPB, b + 1 + (s + 1) // SPB)

            def finish_sum(f):
                v.wait_ge(acc_taken, SPB * (f + 1))
                v.wait_ge(xt_loaded, 16 * (f + 1))
                step.link(nc.vector.tensor_tensor(osum[0][:, :], osum[0][:, :], osum[1][:, :], ALU.add))
                step.link(nc.vector.tensor_scalar(den[:, 0:HEADS], osum[0][:, D:ROW], TINY, None, ALU.max))
                step.link(nc.vector.reciprocal(den[:, HEADS:2 * HEADS], den[:, 0:HEADS]))

            def finish_divide(f):
                for h in range(HEADS):
                    cols = slice(h * F, (h + 1) * F)
                    ins = nc.vector.scalar_tensor_tensor(xt[:, cols], osum[0][:, cols], den[:, HEADS + h:HEADS + h + 1],
                                                         xt[:, cols], ALU.mult, ALU.add)
                    if h < HEADS - 1:
                        step.link(ins)
                ins.then_inc(osum_free, 1)
                v.wait_ge(osum_free, f + 1)

            def finish_stats(f):
                finish_divide(f)
                norm_stats(xt[:, :])

            def finish_norm(f):
                norm(ln_ready, f + 1)

            def finish_residual(f):
                v.wait_ge(h_ready, f + 1)
                if not isinstance(f, int) or f > 0:
                    v.wait_ge(out_stored, 16 * f)
                nc.vector.tensor_tensor(yo[:, :], xt[:, :], bias_b[:, :], ALU.add).then_inc(xt_free, 1)
                v.wait_ge(xt_free, f + 1)

            def finish_lo(f):
                v.wait_ge(hT_hi_ready, 2 * (f + 1))
                for j in range(2):
                    nc.vector.tensor_tensor(hT_lo[:, 0, 512 * j:512 * j + 512], tb[j][:, :],
                                            hT_hi[:, 0, 512 * j:512 * j + 512], ALU.subtract
                                            ).then_inc(hT_lo_ready, 1)

            def finish_halves(f):
                finish_residual(f)
                finish_lo(f)

            def finish_out(f, j):
                v.wait_ge(y_ready, 2 * f + j + 1)
                nc.vector.tensor_tensor(yo[:, 512 * j:512 * j + 512], tb[j][:, :], yo[:, 512 * j:512 * j + 512],
                                        ALU.add).then_inc(y_taken, 1)

            def attend_block(b, first=False, second=False):
                for s in range(SPB):
                    if not (first and s == 0):
                        scores(b, s)
                    weigh(b, s)
                    if first and s == 0:
                        weights_lo(WBLOCKS - 1)
                    if s in (1, 2) and not first and not second:
                        finish_out(b - 2, s - 1)
                    if not first:
                        (finish_sum, finish_stats, finish_norm, finish_halves)[s](b - 1)

            def general_place(w, q):
                step.link(nc.vector.tensor_scalar(near[:, 0:GC], all_dst[:, bass.ds(w * GC, GC)],
                                                  thr[:, bass.ds(q, 1)], None, ALU.subtract))

            def general_weights(q, w):
                n = q * GSTEPS + w
                general_place(w, q)
                v.wait_ge(g_used, n * GC + 4)
                step.link(nc.vector.tensor_tensor(
                    own[:, 0:GC, :], iota_d[:, None, :].to_broadcast([P, GC, SUB]),
                    near[:, 0:GC].unsqueeze(2).to_broadcast([P, GC, SUB]), ALU.is_equal))
                for j in range(3):
                    nc.vector.tensor_tensor(
                        pick_dst[0][:, 0:GC, j, :], own[:, 0:GC, :],
                        all_part[j][:, bass.ds(w * GC, GC)].unsqueeze(2).to_broadcast([P, GC, SUB]), ALU.mult
                    ).then_inc(g_dst_ready, 1)
                for c in range(GC):
                    v.wait_ge(g_used, n * GC + c + 1)
                    nc.vector.tensor_scalar(pick_src[c % 4], iota_src, all_src[:, bass.ds(w * GC + c, 1)], None,
                                            ALU.is_equal).then_inc(g_src_ready, 1)

            def general_scores(n, w, q, s):
                v.wait_ge(g_cleared, n + 1)
                general_place(w, q)
                step.link(nc.vector.tensor_scalar(near[:, GC:2 * GC], near[:, 0:GC], 0.0, float(FARSRC),
                                                  ALU.is_lt, ALU.mult))
                step.link(nc.vector.tensor_scalar(near[:, 2 * GC:3 * GC], near[:, 0:GC], float(SUB - 1), float(FARSRC),
                                                  ALU.is_gt, ALU.mult))
                step.link(nc.vector.tensor_tensor(near[:, GC:2 * GC], near[:, GC:2 * GC], near[:, 2 * GC:3 * GC],
                                                  ALU.add))
                nc.vector.tensor_tensor(idxr[:, 0, 0:GC], near[:, GC:2 * GC], all_src[:, bass.ds(w * GC, GC)], ALU.add
                                        ).then_inc(g_idx_ready, 1)
                v.wait_ge(g_idx_ready, n + 1)
                step.link(nc.vector.tensor_tensor(
                    outside[:, 0:GC, :], iota_d[:, None, :].to_broadcast([P, GC, SUB]),
                    near[:, 0:GC].unsqueeze(2).to_broadcast([P, GC, SUB]), ALU.not_equal))
                step.link(nc.vector.tensor_scalar(outside[:, 0:GC, :], outside[:, 0:GC, :], MASKED, None, ALU.mult))
                step.link(nc.vector.tensor_tensor(
                    query[:, 0:GC], outside[:, 0:GC, :].unsqueeze(2).to_broadcast([P, GC, HEADS, SUB]),
                    er_b[:, s, :].rearrange("p (d h) -> p h d", h=HEADS).unsqueeze(1).to_broadcast(
                        [P, GC, HEADS, SUB]), ALU.add))
                v.wait_ge(g_gathered, 16 * GC)
                v.sem_inc(g_seen, 1)
                el = rows[:, 0, 0:GC, D:ROW].unsqueeze(3).to_broadcast([P, GC, HEADS, SUB])
                nc.vector.tensor_tensor(score[:, 0:GC], query[:, 0:GC], el, ALU.add).then_inc(g_score, 1)
                v.wait_ge(g_score, n + 1)
                sc = score[:, 0:GC]
                step.link(nc.vector.scalar_tensor_tensor(sc, sc, SLOPE, sc, ALU.mult, ALU.max))

            def general_max(b, s, w):
                q = SPB * b + s
                general_scores(2 * q * GSTEPS + w, w, q, s)
                step.link(nc.vector.tensor_reduce(step_max, score[:, 0:GC].rearrange("p c h d -> p (h d) c"),
                                                  AX.X, ALU.max))
                step.link(nc.vector.tensor_tensor(rowmax, rowmax, step_max, ALU.max))

            def general_probs(b, s, w):
                q = SPB * b + s
                n = q * GSTEPS + w
                general_scores((2 * q + 1) * GSTEPS + w, w, q, s)
                nc.vector.tensor_tensor(
                    score[:, 0:GC], score[:, 0:GC],
                    turn[:, P:2 * P].rearrange("p (h d) -> p h d", h=HEADS).unsqueeze(1).to_broadcast(
                        [P, GC, HEADS, SUB]), ALU.subtract).then_inc(g_logits, 1)
                v.wait_ge(g_exp, n + 1)
                nc.vector.tensor_tensor(upper[0][:, 0:GC, :, SUB:], prob[0][:, 0:GC], upper[0][:, 0:GC, :, 0:SUB],
                                        ALU.subtract).then_inc(g_prob_lo, 1)
                v.wait_ge(g_added, n + 1)

            def looped(start, end, per, body):
                nonlocal step
                keep, n0 = step, step.base + step.n
                v.sem_inc(dve_turn, 1)
                with v.Fori(start, end) as i:
                    step = Chain(v, dve_done, n0 + (i - start) * per)
                    body(i)
                    assert step.n == per, step.n
                step = keep
                step.n += per * (end - start)

            def general_weights_block(kb):
                for s in range(SPB):
                    looped(0, GSTEPS, G_WEIGHT_LINKS, lambda w: general_weights(SPB * kb + s, w))
                weights_lo(kb)
                v.wait_ge(w1_lo_ready, 2 * (kb + 1))

            def general_block(b):
                for s in range(SPB):
                    q = SPB * b + s
                    v.wait_ge(er_loaded[s], 16 * (b + 1))
                    step.link(nc.vector.memset(rowmax, FLOOR))
                    looped(0, GSTEPS, G_MAX_LINKS, lambda w: general_max(b, s, w))
                    nc.vector.tensor_copy(rowmax, rowmax).then_inc(rowmax_ready, 1)
                    spread_diag(q)
                    v.wait_ge(max_spread, q + 1)
                    looped(0, GSTEPS, G_PROB_LINKS, lambda w: general_probs(b, s, w))
                finish_sum(b)
                finish_stats(b)
                finish_norm(b)
                finish_halves(b)
                finish_out(b, 0)
                finish_out(b, 1)
                v.wait_ge(y_taken, 2 * (b + 1))
                v.sem_inc(g_block_free, 1)

            fit, linked = fits(v), step.n
            with v.If(fit):
                weights_block(0, first=True)
                outer, n0 = step, step.n
                with v.Fori(1, WBLOCKS) as kb:
                    step = Chain(v, dve_done, n0 + (kb - 1) * SPB)
                    weights_block(kb)
                    assert step.n == SPB
                step = outer
                step.n = n0 + SPB * (WBLOCKS - 1)
                v.wait_ge(picks_used, C * NWSUB)
                make_outside(0)
                make_query(0, 0, 1)
                scores(0, 0)
                attend_block(0, first=True)
                attend_block(1, second=True)
                outer, n0 = step, step.n
                with v.Fori(2, TILES) as b:
                    step = Chain(v, dve_done, n0 + (b - 2) * BLOCK_LINKS)
                    attend_block(b)
                    assert step.n == BLOCK_LINKS, step.n
                step = outer
                step.n = n0 + BLOCK_LINKS * (TILES - 2)
                finish_sum(TILES - 1)
                finish_stats(TILES - 1)
                finish_norm(TILES - 1)
                finish_out(TILES - 2, 0)
                finish_out(TILES - 2, 1)
                finish_lo(TILES - 1)
                finish_residual(TILES - 1)
                finish_out(TILES - 1, 0)
                finish_out(TILES - 1, 1)
            with v.Else():
                step.n = linked
                v.wait_ge(all_loaded, 48)
                step.link(nc.vector.memset(zeros_b, 0.0))
                step.link(nc.vector.tensor_copy(all_dst, all_i[:, 0:COLS]))
                step.link(nc.vector.tensor_copy(all_src, all_i[:, COLS:]))
                split_weights(all_w, all_part, all_res)
                nc.vector.memset(rows[:, 0, :, :], 0.0).then_inc(all_ready, 1)
                v.wait_ge(all_ready, 1)
                looped(0, WBLOCKS, SPB * GSTEPS * G_WEIGHT_LINKS, general_weights_block)
                v.sem_inc(g_block_free, 1)
                general_block(0)
                looped(1, TILES, G_BLOCK_LINKS, general_block)

        @block.scalar
        def _(act):
            def relu_norm(xs, ready):
                nc.scalar.activation(hb[:, :], xs, ACT.Relu, bias=rs[:, 1:2], scale=rs[:, 0:1]).then_inc(ready, 1)

            def w_top(k0, k1):
                for k in range(k0, k1):
                    act.wait_ge(w_loaded[k], 16)
                    nc.scalar.copy(w_hi[:, k, :], w_in[:, k, :]).then_inc(w_hi_ready, 1)

            def z_h(t, slot):
                act.wait_ge(z_ln_ready, t + 1)
                if not isinstance(t, int) or t > 0:
                    act.wait_ge(z_hT_ready, t)
                relu_norm(xz[slot][:, :], z_h_ready)

            def z_hi(t, slot):
                act.wait_ge(z_hT_ready, t + 1)
                if not isinstance(t, int) or t > 1:
                    act.wait_ge(z_ready, t - 1)
                for j in range(2):
                    nc.scalar.copy(hT_hi[:, slot, 512 * j:512 * j + 512], tb[j][:, :]).then_inc(z_hi_ready, 1)

            def z_top(t, slot, use):
                act.wait_ge(z_ready, t + 1)
                if not isinstance(use, int) or use > 1:
                    act.wait_ge(z_stored[slot], 32 * (use - 1))
                nc.scalar.copy(zt[slot][:, 0:512].bitcast(BF16), acc[slot][:, :]).then_inc(z_top_ready, 1)

            z_h(0, 0)
            w_top(0, 2)
            z_hi(0, 0)
            z_h(1, 1)
            w_top(2, KD)
            z_hi(1, 1)
            z_h(2, 0)

            def z_pair(g):
                for s in range(2):
                    t = 2 * g + s
                    z_top(t - 2, s, g)
                    z_hi(t, s)
                    z_h(t + 1, 1 - s)

            z_pair(1)
            with act.Fori(2, TILES // 2 - 1) as g:
                z_pair(g)
            z_top(TILES - 4, 0, TILES // 2 - 1)
            z_hi(TILES - 2, 0)
            z_h(TILES - 1, 1)
            z_top(TILES - 3, 1, TILES // 2 - 1)
            z_hi(TILES - 1, 1)
            z_top(TILES - 2, 0, TILES // 2)
            z_top(TILES - 1, 1, TILES // 2)

            def weights_hi(kb):
                act.wait_ge(wblock_ready, kb + 1)
                for j in range(2):
                    cols = slice(512 * j, 512 * j + 512)
                    nc.scalar.copy(w1_hi[:, bass.ds(kb, 1), cols], wblock[:, cols].unsqueeze(1)
                                   ).then_inc(w1_hi_ready, 1)

            def copy_parts(at, s):
                for j in range(3):
                    ins = nc.scalar.copy(part_sum[j][SUB * s:SUB * (s + 1), :], at[SUB * j:SUB * (j + 1), :])
                ins.then_inc(part_copied, 1)

            def weights_block(kb, first=False):
                for s in range(SPB):
                    q = SPB * kb + s
                    act.wait_ge(picks_used, C * (q + 1))
                    if s == 0 and not first:
                        act.wait_ge(wblock_ready, kb)
                    copy_parts(acc[s % 2], s)
                    if s == 1 and not first:
                        weights_hi(kb - 1)

            def probs(b, s):
                q, sl = SPB * b + s, s % 2
                if not isinstance(q, int) or q > 1:
                    act.wait_ge(acc_ready, q - 1)
                for g in range(GROUPS):
                    cs = slice(g * GCH, (g + 1) * GCH)
                    act.wait_ge(logits_ready, GROUPS * q + g + 1)
                    nc.scalar.activation(prob[sl][:, cs], score[:, cs], ACT.Exp).then_inc(exp_done, 1)

            def scale_outside(q):
                act.wait_ge(outside_ready, q + 1)
                nc.scalar.mul(outside, outside, MASKED).then_inc(outside_scaled, 1)

            def copy_acc(q, s, block_free, slot=None):
                act.wait_ge(acc_ready, q + 1)
                if block_free is not None:
                    act.wait_ge(osum_free, block_free)
                at = acc[s % 2 if slot is None else slot]
                for t in range(2):
                    o = osum[t][SUB * s:SUB * (s + 1), :]
                    nc.scalar.copy(o[:, 0:D], at[SUB * t:SUB * (t + 1), :])
                    ins = nc.scalar.copy(o[:, D:ROW], small[SUB * t:SUB * (t + 1), 0:HEADS])
                ins.then_inc(acc_taken, 1)

            def finish_h(f):
                act.wait_ge(ln_ready, f + 1)
                if not isinstance(f, int) or f > 0:
                    act.wait_ge(hT_ready, f)
                relu_norm(xt[:, :], h_ready)

            def finish_hi(f):
                act.wait_ge(hT_ready, f + 1)
                if not isinstance(f, int) or f > 0:
                    act.wait_ge(y_ready, 2 * f)
                for j in range(2):
                    nc.scalar.copy(hT_hi[:, 0, 512 * j:512 * j + 512], tb[j][:, :]).then_inc(hT_hi_ready, 1)

            def attend_block(b, first=False):
                for s in range(SPB):
                    q = SPB * b + s
                    if s == 3 and not first:
                        finish_h(b - 1)
                    scale_outside(q + 1)
                    probs(b, s)
                    if s == 3 and not first:
                        finish_hi(b - 1)
                    if not (first and s == 0):
                        copy_acc(q - 1, (s - 1) % SPB, b if s == 1 and not first else None)

            def general_weights_hi(kb):
                for s in range(SPB):
                    act.wait_ge(g_part_ready, SPB * kb + s + 1)
                    copy_parts(acc[0], s)
                weights_hi(kb)

            def general_probs(q, w):
                n = q * GSTEPS + w
                act.wait_ge(g_logits, n + 1)
                nc.scalar.activation(prob[0][:, 0:GC], score[:, 0:GC], ACT.Exp).then_inc(g_exp, 1)

            def general_block(b):
                for s in range(SPB):
                    q = SPB * b + s
                    with act.Fori(0, GSTEPS) as w:
                        general_probs(q, w)
                    copy_acc(q, s, None, 0)
                finish_h(b)
                finish_hi(b)

            act.wait_ge(z_stored[0], 32 * (TILES // 2))
            act.wait_ge(z_stored[1], 32 * (TILES // 2))
            fit = fits(act)
            with act.If(fit):
                weights_block(0, first=True)
                with act.Fori(1, WBLOCKS) as kb:
                    weights_block(kb)
                scale_outside(0)
                weights_hi(WBLOCKS - 1)
                attend_block(0, first=True)
                with act.Fori(1, TILES) as b:
                    attend_block(b)
                copy_acc(NSUB - 1, SPB - 1, None)
                finish_h(TILES - 1)
                finish_hi(TILES - 1)
            with act.Else():
                with act.Fori(0, WBLOCKS) as kb:
                    general_weights_hi(kb)
                general_block(0)
                with act.Fori(1, TILES) as b:
                    general_block(b)

        @block.tensor
        def _(pe):
            mm = nc.tensor.matmul
            pe.wait_ge(const_ready, 1)
            def turn_h(ready):
                for k in range(KD):
                    ins = nc.tensor.transpose(tb[k // 4][:, (k % 4) * P:(k % 4 + 1) * P], hb[:, k * P:(k + 1) * P],
                                              ident[:, :])
                ins.then_inc(ready, 1)

            def z_turn(t):
                pe.wait_ge(z_h_ready, t + 1)
                if not isinstance(t, int) or t > 0:
                    pe.wait_ge(z_lo_ready, 2 * t)
                turn_h(z_hT_ready)

            def product(to, cols, slot, hi, lo, first=False):
                n = 0
                for k in range(KD):
                    if first:
                        pe.wait_ge(w_lo_ready, k + 1)
                    hh, hl = (t[:, slot, k * P:(k + 1) * P] for t in (hT_hi, hT_lo))
                    for a, w in ((hh, hi), (hh, lo), (hl, hi)):
                        ins = mm(to, a, w[:, k, cols], start=(n == 0), stop=(n == 3 * KD - 1))
                        n += 1
                return ins

            def z_product(t, slot, use):
                pe.wait_ge(z_lo_ready, 2 * (t + 1))
                if not isinstance(use, int) or use > 1:
                    pe.wait_ge(z_row_ready, t - 1)
                product(acc[slot][:, 0:512], slice(0, 512), slot, w_hi, w_lo, isinstance(t, int) and t == 0)
                product(acc[slot][:, 512:1024], slice(512, 1024), slot, w_hi, w_lo).then_inc(z_ready, 1)

            z_turn(0)
            pe.wait_ge(picks_ready, 1)
            mm(acc[0][0:NSUB, 0:512], pick[:, :], edges_f[:, 1:513], start=True, stop=True)
            mm(acc[0][0:NSUB, 512:COLS], pick[:, :], edges_f[:, 513:COLS + 1], start=True, stop=True)
            mm(small[0:NSUB, 0:1], notge[:, :], ones[:, 0:1], start=True, stop=True, skip_group_check=True)
            mm(small[0:NSUB, 8:9], thr[0:1, :], ones[0:1, 0:1], start=True, stop=True, skip_group_check=True
               ).then_inc(rows_picked, 1)
            pe.wait_ge(counts_ready, 1)
            mm(turn[0:1, 0:NSUB], cnt[0:NSUB, 2:3], ident[0:NSUB, 0:NSUB], start=True, stop=True,
               skip_group_check=True)
            mm(turn[0:1, 128:129], cnt[:, 0:1], ones[:, 0:1], start=True, stop=True, skip_group_check=True
               ).then_inc(counts_turned, 1)

            z_turn(1)
            z_product(0, 0, 1)
            z_turn(2)
            z_product(1, 1, 1)
            with pe.Fori(1, TILES // 2 - 1) as g:
                for s in range(2):
                    z_turn(2 * g + 1 + s)
                    z_product(2 * g + s, s, g + 1)
            z_turn(TILES - 1)
            z_product(TILES - 2, 0, TILES // 2)
            z_product(TILES - 1, 1, TILES // 2)

            def weights_block(kb, first=False):
                for s in range(SPB):
                    q = SPB * kb + s
                    pe.wait_ge(pick_dst_ready, q + 1)
                    if not first or s >= 2:
                        pe.wait_ge(part_copied, q - 1)
                    for c in range(C):
                        pe.wait_ge(pick_src_ready, C * q + c + 1)
                        for j in range(2):
                            ins = mm(acc[s % 2][0:96, 512 * j:512 * j + 512],
                                     pick_dst[s % 2][:, c, :, :].rearrange("p j d -> p (j d)"),
                                     pick_src[(C * s + c) % 4][:, 512 * j:512 * j + 512],
                                     start=(c == 0), stop=(c == C - 1))
                        ins.then_inc(picks_used, 1)

            def attend(q, s, c0, c1):
                sl = s % 2
                for c in range(c0, c1):
                    if c % GCH == 0:
                        pe.wait_ge(prob_lo_ready, GROUPS * q + c // GCH + 1)
                    z2 = rows[:, sl, c, 0:D].bitcast(BF16)
                    for h in range(HEADS):
                        pw = upper[sl][:, c, h, :]
                        to = acc[sl][0:2 * SUB, h * F:(h + 1) * F]
                        for t in range(2):
                            ins = mm(to, pw, z2[:, t * D + h * F:t * D + (h + 1) * F],
                                     start=(c == 0 and t == 0 and h % 2 == 0),
                                     stop=(c == C - 1 and t == 1 and h % 2 == 1), skip_group_check=True)
                    ins.then_inc(rows_used, 1)

            def attend_sums(q, s, first=False):
                if not first:
                    pe.wait_ge(acc_taken, q)
                for c in range(C):
                    for h in range(HEADS):
                        ins = mm(small[0:2 * SUB, h:h + 1], upper[s % 2][:, c, h, :],
                                 ones_b[:, 0:1], start=(c == 0 and h == 0), stop=(c == C - 1 and h == HEADS - 1),
                                 skip_group_check=True)
                ins.then_inc(acc_ready, 1)

            def turn_rowmax(q):
                pe.wait_ge(rowmax_ready, q + 1)
                nc.tensor.transpose(turn[:, 0:P], rowmax, ident[:, :]).then_inc(rowmax_turned, 1)

            def spread_max(q):
                pe.wait_ge(diag_ready, q + 1)
                mm(turn[:, P:2 * P], ones[:, :], diag, start=True, stop=True).then_inc(max_spread, 1)

            def finish_turn(f):
                pe.wait_ge(h_ready, f + 1)
                if not isinstance(f, int) or f > 0:
                    pe.wait_ge(y_taken, 2 * f)
                turn_h(hT_ready)

            def finish_product(f, part):
                pe.wait_ge(hT_lo_ready, 2 * (f + 1))
                c0 = part * (D // 4)
                ins = product(tb[part // 2][:, c0 % 512:c0 % 512 + D // 4], slice(c0, c0 + D // 4), 0, w1_hi, w1_lo)
                if part % 2:
                    ins.then_inc(y_ready, 1)

            def attend_block(b, first=False, second=False):
                for s in range(SPB):
                    q, before = SPB * b + s, (s - 1) % SPB
                    ended = not first and not second
                    run = not (first and s == 0)
                    if run:
                        if not first or s >= 3:
                            pe.wait_ge(acc_taken, q - 2)
                        attend(q - 1, before, 0, C)
                        attend_sums(q - 1, before, first and s == 1)
                    if s == 2 and ended:
                        finish_product(b - 2, 2)
                    turn_rowmax(q)
                    spread_max(q)
                    if s < 3 and ended:
                        finish_product(b - 2, (0, 1, 3)[s])
                    if s == 3 and not first:
                        finish_turn(b - 1)

            def add_zero(to, start):
                return mm(to, zeros_b[:, 0:to.shape[0]], zeros_b[:, 0:to.shape[1]], start=start, stop=not start,
                          skip_group_check=True)

            def general_weights_block(kb):
                for s in range(SPB):
                    q = SPB * kb + s
                    for j in range(2):
                        add_zero(acc[0][0:96, 512 * j:512 * j + 512], True)
                    with pe.Fori(0, GSTEPS) as w:
                        n = q * GSTEPS + w
                        pe.wait_ge(g_dst_ready, 3 * (n + 1))
                        for c in range(GC):
                            pe.wait_ge(g_src_ready, GC * n + c + 1)
                            for j in range(2):
                                ins = mm(acc[0][0:96, 512 * j:512 * j + 512],
                                         pick_dst[0][:, c, :, :].rearrange("p j d -> p (j d)"),
                                         pick_src[c % 4][:, 512 * j:512 * j + 512],
                                         start=False, stop=False, skip_group_check=True)
                            ins.then_inc(g_used, 1)
                    add_zero(acc[0][0:96, 0:512], False)
                    add_zero(acc[0][0:96, 512:1024], False).then_inc(g_part_ready, 1)
                    pe.wait_ge(part_copied, q + 1)

            def general_block(b):
                for s in range(SPB):
                    q = SPB * b + s
                    turn_rowmax(q)
                    spread_max(q)
                    sums = [acc[0][0:2 * SUB, 0:512], acc[0][0:2 * SUB, 512:1024], small[0:2 * SUB, 0:HEADS]]
                    for to in sums:
                        add_zero(to, True)
                    with pe.Fori(0, GSTEPS) as w:
                        n = q * GSTEPS + w
                        pe.wait_ge(g_prob_lo, n + 1)
                        for c in range(GC):
                            z2 = rows[:, 0, c, 0:D].bitcast(BF16)
                            for h in range(HEADS):
                                pw = upper[0][:, c, h, :]
                                for t in range(2):
                                    mm(acc[0][0:2 * SUB, h * F:(h + 1) * F], pw,
                                       z2[:, t * D + h * F:t * D + (h + 1) * F], start=False, stop=False,
                                       skip_group_check=True)
                                ins = mm(small[0:2 * SUB, h:h + 1], pw, ones_b[:, 0:1], start=False, stop=False,
                                         skip_group_check=True)
                        ins.then_inc(g_added, 1)
                    for to in sums:
                        ins = add_zero(to, False)
                    ins.then_inc(acc_ready, 1)
                    pe.wait_ge(acc_taken, q + 1)
                finish_turn(b)
                for part in range(4):
                    finish_product(b, part)

            pe.wait_ge(z_row_ready, TILES)
            fit = fits(pe)
            with pe.If(fit):
                weights_block(0, first=True)
                with pe.Fori(1, WBLOCKS) as kb:
                    weights_block(kb)
                pe.wait_ge(part_copied, NWSUB)
                attend_block(0, first=True)
                attend_block(1, second=True)
                with pe.Fori(2, TILES) as b:
                    attend_block(b)
                pe.wait_ge(acc_taken, NSUB - 2)
                attend(NSUB - 1, SPB - 1, 0, C)
                attend_sums(NSUB - 1, SPB - 1)
                for part in range(4):
                    finish_product(TILES - 2, part)
                finish_turn(TILES - 1)
                for part in range(4):
                    finish_product(TILES - 1, part)
            with pe.Else():
                pe.wait_ge(all_ready, 1)
                pe.sem_inc(g_used, 4)
                with pe.Fori(0, WBLOCKS) as kb:
                    general_weights_block(kb)
                general_block(0)
                with pe.Fori(1, TILES) as b:
                    general_block(b)


_INS = ['x', 'src', 'dst', 'edge_weight', 'L0_gnn_W', 'L0_gnn_a_l', 'L0_gnn_a_r', 'L1_gnn_bias']


def kernel(**inputs):
    import numpy as np
    import concourse.bacc as bacc
    from concourse.bass_utils import run_bass_kernel_spmd as run

    nc = bacc.Bacc("TRN2", target_bir_lowering=False, num_devices=1)
    arrays, args = {}, []
    for name in _INS:
        a = np.ascontiguousarray(inputs[name])
        arrays[f"in_{name}"] = a
        args.append(nc.dram_tensor(f"in_{name}", a.shape, mybir.dt.from_np(a.dtype), kind="ExternalInput").ap())
    out = nc.dram_tensor("out", (N, D), FP32, kind="ExternalOutput").ap()
    gnn_kernel(nc, *args, out)
    r = run(nc, [arrays], core_ids=[0])
    return r.results[0]["out"]
```
